# Optimizing a Trainium2 kernel written in Bass

```python
import numpy as np
import jax
import jax.numpy as jnp

def _softmax(x, axis=-1):
    return jax.nn.softmax(x, axis=axis)
def _gelu(x):
    return jax.nn.gelu(x, approximate=True)
def _silu(x):
    return jax.nn.silu(x)
def _sigmoid(x):
    return jax.nn.sigmoid(x)
def _layernorm(x, axis=-1, eps=1e-5):
    m = jnp.mean(x, axis=axis, keepdims=True)
    v = jnp.var(x, axis=axis, keepdims=True)
    return (x - m) / jnp.sqrt(v + eps)
def _scatter_add(tgt, idx, src, axis=0):
    return tgt.at[idx].add(src)
def _segment_sum(src, seg, n):
    return jax.ops.segment_sum(src, seg, n)

kernel_name = 'mk_conv_seq_d2_conv_nchw16_375fdd'

def setup_inputs(seed: int = 0):
    np.random.seed(seed)
    _w = jnp.asarray
    def _rec_inputs():
        import jax
        import jax.numpy as jnp
        _gk = jax.random.key(seed)
        x = -0.000125 + 0.9999 * jax.random.normal(jax.random.fold_in(_gk, 1), (32, 16, 256, 256), jnp.float32)
        return x
    x = _rec_inputs()
    def _L0_conv_setup():
        import jax, jax.numpy as jnp
        import numpy as np
        C = 16
        HID = 128
        B, H, W = (32, 256, 256)
        key = jax.random.key(seed)
        ks = jax.random.split(key, 6)
        x = jax.random.normal(ks[0], (B, C, H, W), dtype=jnp.float32)
        conv_w = jax.random.normal(ks[1], (C, C, 3, 3), dtype=jnp.float32) * (1.0 / np.sqrt(C * 9))
        w1 = jax.random.normal(ks[2], (HID, C), dtype=jnp.float32) * (1.0 / np.sqrt(C))
        b1 = jax.random.normal(ks[3], (HID,), dtype=jnp.float32) * 0.01
        w2 = jax.random.normal(ks[4], (C, HID), dtype=jnp.float32) * (1.0 / np.sqrt(HID))
        b2 = jax.random.normal(ks[5], (C,), dtype=jnp.float32) * 0.01
        return {'x': x, 'conv_w': conv_w, 'w1': w1, 'b1': b1, 'w2': w2, 'b2': b2}
    _L0_conv_all = _L0_conv_setup()
    _L0_conv_in = {k: v for k, v in _L0_conv_all.items() if k in ('conv_w', 'w1', 'b1', 'w2', 'b2', )}
    del _L0_conv_all

    def _L1_conv_setup():
        import jax, jax.numpy as jnp
        import numpy as np

        def _conv2d_same(x, w, b):
            y = jax.lax.conv_general_dilated(x, w, window_strides=(1, 1), padding=((1, 1), (1, 1)), dimension_numbers=('NCHW', 'OIHW', 'NCHW'))
            return y + b[None, :, None, None]
        key = jax.random.key(seed)
        ks = jax.random.split(key, 5)
        B, C, H, W = (16, 16, 512, 512)
        K = 3
        bound = float(np.sqrt(1.0 / (C * K * K)))
        x = jax.random.normal(ks[0], (B, C, H, W), dtype=jnp.float32)
        w1 = jax.random.uniform(ks[1], (C, C, K, K), minval=-bound, maxval=bound, dtype=jnp.float32)
        b1 = jax.random.uniform(ks[2], (C,), minval=-bound, maxval=bound, dtype=jnp.float32)
        w2 = jax.random.uniform(ks[3], (C, C, K, K), minval=-bound, maxval=bound, dtype=jnp.float32)
        b2 = jax.random.uniform(ks[4], (C,), minval=-bound, maxval=bound, dtype=jnp.float32)
        return {'x': x, 'w1': w1, 'b1': b1, 'w2': w2, 'b2': b2}
    _L1_conv_all = _L1_conv_setup()
    _L1_conv_in = {k: v for k, v in _L1_conv_all.items() if k in ('w1', 'b1', 'w2', 'b2', )}
    del _L1_conv_all

    return {
        "x": x,
        "L0_conv_conv_w": _L0_conv_in["conv_w"],
        "L0_conv_w1": _L0_conv_in["w1"],
        "L0_conv_b1": _L0_conv_in["b1"],
        "L0_conv_w2": _L0_conv_in["w2"],
        "L0_conv_b2": _L0_conv_in["b2"],
        "L1_conv_w1": _L1_conv_in["w1"],
        "L1_conv_b1": _L1_conv_in["b1"],
        "L1_conv_w2": _L1_conv_in["w2"],
        "L1_conv_b2": _L1_conv_in["b2"],
    }

def reference(x, L0_conv_conv_w, L0_conv_w1, L0_conv_b1, L0_conv_w2, L0_conv_b2, L1_conv_w1, L1_conv_b1, L1_conv_w2, L1_conv_b2):
    import jax
    import jax.numpy as jnp
    def _L0_conv_ref(x, conv_w, w1, b1, w2, b2):
        import jax, jax.numpy as jnp
        import numpy as np
        C = 16
        HID = 128
        B, H, W = (32, 256, 256)
        y = jax.lax.conv_general_dilated(x, conv_w, window_strides=(1, 1), padding=((1, 1), (1, 1)), dimension_numbers=('NCHW', 'OIHW', 'NCHW'))
        h = jax.nn.relu(jnp.einsum('bchw,kc->bkhw', y, w1) + b1[None, :, None, None])
        upd = jnp.einsum('bkhw,ck->bchw', h, w2) + b2[None, :, None, None]
        return x + upd

    def _L1_conv_ref(x, w1, b1, w2, b2):
        import jax, jax.numpy as jnp
        import numpy as np

        def _conv2d_same(x, w, b):
            y = jax.lax.conv_general_dilated(x, w, window_strides=(1, 1), padding=((1, 1), (1, 1)), dimension_numbers=('NCHW', 'OIHW', 'NCHW'))
            return y + b[None, :, None, None]
        out = _conv2d_same(x, w1, b1)
        out = jax.nn.relu(out)
        out = _conv2d_same(out, w2, b2)
        return out + x

    def _gn(v, G=8, eps=1e-5):
        B_, C_, H_, W_ = v.shape
        g = v.reshape(B_, G, C_ // G, H_, W_)
        m = jnp.mean(g, axis=(2, 3, 4), keepdims=True)
        s = jnp.var(g, axis=(2, 3, 4), keepdims=True)
        return ((g - m) / jnp.sqrt(s + eps)).reshape(v.shape)

    def _ln_c(v, eps=1e-6):
        m = jnp.mean(v, axis=1, keepdims=True)
        s = jnp.var(v, axis=1, keepdims=True)
        return (v - m) / jnp.sqrt(s + eps)

    def _ln_t(v, eps=1e-5):
        m = jnp.mean(v, axis=-1, keepdims=True)
        s = jnp.var(v, axis=-1, keepdims=True)
        return (v - m) / jnp.sqrt(s + eps)

    def _to_tokens(v):
        B_, C_, H_, W_ = v.shape
        return v.reshape(B_, C_, H_ * W_).transpose(0, 2, 1)
    def _from_tokens(t, like):
        B_, C_, H_, W_ = like.shape
        return t.transpose(0, 2, 1).reshape(B_, C_, H_, W_)

    x = _L0_conv_ref(x, L0_conv_conv_w, L0_conv_w1, L0_conv_b1, L0_conv_w2, L0_conv_b2)
    x = _L1_conv_ref(x, L1_conv_w1, L1_conv_b1, L1_conv_w2, L1_conv_b2)
    return x


_drawn_inputs = setup_inputs


def setup_inputs(seed=0):
    import zlib

    import numpy as np

    out = dict(_drawn_inputs(seed))
    spreads = {}
    factors = {'L0_conv_b1': 8.0, 'L0_conv_b2': 7.696, 'L1_conv_b1': 4.333}
    for name, (base, spread) in spreads.items():
        noise = np.random.default_rng([zlib.crc32(name.encode()), seed]).standard_normal(out[name].shape)
        drawn = base * np.exp(spread * noise) if base else spread * noise
        out[name] = jnp.asarray(drawn.astype(out[name].dtype))
    for name, factor in factors.items():
        out[name] = (out[name] * factor).astype(out[name].dtype)
    return out
```

```python
import numpy as np
import concourse.bass as bass
import concourse.mybir as mybir
from contextlib import ExitStack

IMAGES, CH, H, W = 32, 16, 256, 256
HID = 128
SIDE = 2
PAIRS = IMAGES // SIDE
ROWS = 6
PITCH = H + 2
STEPS = PAIRS * PITCH // ROWS
WP = W + 2
QUAD = 32
P = 128
TAPS = 3
NEW = ROWS * CH
STACKED = 4
assert PITCH % ROWS == 0 and STEPS % 2 == 0


def build_program(nc, xt, conv0_w, conv1_w, conv2_w, mix1_w, mix2_w, mix1_b, x1_b, c1_b, out_b,
                  x1_mask, c1_mask, out):
    f32, f32r = mybir.dt.float32, mybir.dt.float32r
    ALU, ACT = mybir.AluOpType, mybir.ActivationFunctionType
    with ExitStack() as ctx:
        def sbuf(name, shape, dt=f32):
            return ctx.enter_context(nc.sbuf_tensor(name, shape, dt))

        def sem(name):
            return ctx.enter_context(nc.semaphore(name))

        conv0 = sbuf("conv0", [P, TAPS, NEW])
        conv1 = sbuf("conv1", [P, TAPS, NEW])
        conv2 = sbuf("conv2", [P, TAPS, P])
        mix1_raw = sbuf("mix1_raw", [P, ROWS, HID])
        mix1_hi = sbuf("mix1_hi", [P, ROWS, HID], f32r)
        mix1_lo = sbuf("mix1_lo", [P, ROWS, HID], f32r)
        mix2 = sbuf("mix2", [P, 2, QUAD])
        mix1_bias = sbuf("mix1_bias", [P, 1])
        x1_bias = sbuf("x1_bias", [P, 1])
        c1_bias = sbuf("c1_bias", [P, 1])
        out_bias = sbuf("out_bias", [P, 1])
        x1_keep = sbuf("x1_keep", [P, STEPS])
        c1_keep = sbuf("c1_keep", [P, STEPS])
        x1_bias_at = sbuf("x1_bias_at", [P, STEPS])
        c1_bias_at = sbuf("c1_bias_at", [P, STEPS])

        x_in = [sbuf(f"x_in{i}", [P, SIDE, WP]) for i in range(2)]
        x_b = [sbuf(f"x_b{i}", [NEW, SIDE, W]) for i in range(2)]
        stack_a = sbuf("stack_a", [P, SIDE * W], f32r)
        stack_b = sbuf("stack_b", [P, SIDE * W], f32r)
        hid = sbuf("hid", [P, ROWS, SIDE * W])
        x1 = [sbuf(f"x1_{i}", [P, SIDE, WP]) for i in range(2)]
        c1 = [sbuf(f"c1_{i}", [P, SIDE, WP]) for i in range(2)]
        out_sb = [sbuf(f"out_sb{i}", [P, SIDE, W]) for i in range(2)]

        y_ps = ctx.enter_context(nc.psum_tensor("y_ps", [P, SIDE * W], f32))
        h_ps = [ctx.enter_context(nc.psum_tensor(f"h_ps{i}", [P, 2, SIDE * W], f32)) for i in range(2)]
        upd_ps = ctx.enter_context(nc.psum_tensor("upd_ps", [P, SIDE * W], f32))
        c1_ps = ctx.enter_context(nc.psum_tensor("c1_ps", [P, SIDE * W], f32))
        c2_ps = ctx.enter_context(nc.psum_tensor("c2_ps", [P, SIDE * W], f32))

        weights_loaded = sem("weights_loaded")
        x_loaded = [sem(f"x_loaded{i}") for i in range(2)]
        stored = [sem(f"stored{i}") for i in range(2)]
        cleared = sem("cleared")
        mix1_split = sem("mix1_split")
        tables_ready = sem("tables_ready")
        y_done = sem("y_done")
        y_hi = sem("y_hi")
        y_lo = sem("y_lo")
        h_done = sem("h_done")
        relu_act = sem("relu_act")
        relu_dve = sem("relu_dve")
        upd_done = sem("upd_done")
        xb_ready = sem("xb_ready")
        x1_ready = sem("x1_ready")
        c1_done = sem("c1_done")
        c1_main = sem("c1_main")
        c1_carry = sem("c1_carry")
        c2_done = sem("c2_done")
        out_ready = sem("out_ready")

        LOADS = 11
        block = ctx.enter_context(nc.Block())

        PEELED = 3
        LOOPS = (STEPS - 1 - PEELED) // 2

        def steps(engine, step, first=0, last=True):
            for t in range(first, PEELED):
                step(t, t % 2, t // 2)
            with engine.Fori(0, LOOPS) as j:
                step(2 * j + PEELED, 1, j + PEELED // 2)
                step(2 * j + PEELED + 1, 0, j + PEELED // 2 + 1)
            if last:
                step(STEPS - 1, 1, (STEPS - 1) // 2)

        def after(t, n):
            return not isinstance(t, int) or t > n

        @block.sync
        def _(sp):
            def load_x(t, b):
                first = t * NEW
                edges = xt[bass.ds(first, 8 * CH), :].rearrange("(r c) w -> r c w", c=CH)[0:8:7]
                sp.dma_start(x_in[b][NEW:P].rearrange("p s w -> p (s w)"),
                             edges).then_inc(x_loaded[b], 16)
                sp.dma_start(x_in[b][0:NEW].rearrange("p s w -> p (s w)"),
                             xt[bass.ds(first + CH, NEW), :]).then_inc(x_loaded[b], 16)

            def store_out(t, b):
                sp.dma_start(out[bass.ds(t * NEW, QUAD), :],
                             out_sb[b][NEW:P].rearrange("p s w -> p (s w)")).then_inc(stored[b], 16)
                sp.dma_start(out[bass.ds(t * NEW + QUAD, NEW - QUAD), :],
                             out_sb[b][0:NEW - QUAD].rearrange("p s w -> p (s w)")).then_inc(stored[b], 16)

            load_x(0, 0)
            for dst, src in ((conv0, conv0_w), (conv1, conv1_w), (conv2, conv2_w), (mix1_raw, mix1_w),
                             (mix2, mix2_w), (mix1_bias, mix1_b), (x1_bias, x1_b), (c1_bias, c1_b),
                             (out_bias, out_b), (x1_keep, x1_mask), (c1_keep, c1_mask)):
                sp.dma_start(dst[:], src).then_inc(weights_loaded, 16)
            load_x(1, 1)

            def step(t, b, half):
                sp.wait_ge(y_done, t)
                sp.wait_ge(xb_ready, t)
                load_x(t + 1, 1 - b)
                sp.wait_ge(out_ready, t)
                store_out(t - 1, 1 - b)

            steps(sp, step, first=1, last=False)
            for t in (STEPS - 1, STEPS):
                sp.wait_ge(out_ready, t)
                store_out(t - 1, (t - 1) % 2)
            for b in range(2):
                sp.wait_ge(stored[b], 32 * (STEPS // 2))

        @block.gpsimd
        def _(pool):
            for tile in (*x1, *c1, stack_a, stack_b):
                view = tile[:] if tile.dtype == f32 else tile[:].bitcast(f32)
                nc.gpsimd.memset(view, 0.0).then_inc(cleared, 1)

        @block.tensor
        def _(pe):
            def conv(ps, weights, src, outs):
                for tap in range(TAPS):
                    last = nc.tensor.matmul(ps[0:outs, :], weights[:, tap, :], src[:, :, tap:tap + W],
                                            start=(tap == 0), stop=(tap == TAPS - 1))
                return last

            def step(t, b, half):
                pe.wait_ge(x_loaded[b], half * 32 + 32)
                if after(t, 0):
                    pe.wait_ge(y_lo, t)
                conv(y_ps, conv0, x_in[b], NEW).then_inc(y_done, 1)
                if after(t, 0):
                    pe.wait_ge(x1_ready, t)
                    if after(t, 1):
                        pe.wait_ge(c1_carry, t - 1)
                    conv(c1_ps, conv1, x1[1 - b], NEW).then_inc(c1_done, 1)
                pe.wait_ge(y_lo, t + 1)
                if not after(t, 0):
                    pe.wait_ge(mix1_split, 2)
                for pair in range(ROWS // 2):
                    if pair == 2:
                        pe.wait_ge(relu_act, 2 * t + 1)
                    elif pair == 1 and after(t, 0):
                        pe.wait_ge(relu_act, 2 * t)
                    elif pair == 0 and after(t, 0):
                        pe.wait_ge(relu_dve, t)
                    for k in range(2):
                        row = 2 * pair + k
                        stack = stack_a if row < STACKED else stack_b
                        dst = h_ps[(pair + b) % 2][:, k, :]
                        nc.tensor.matmul(dst, mix1_hi[:, row, :], stack[:], start=True, stop=False)
                        last = nc.tensor.matmul(dst, mix1_lo[:, row, :], stack[:], start=False, stop=True)
                    last.then_inc(h_done, 1)
                if after(t, 0):
                    pe.wait_ge(c1_main, t)
                    if after(t, 1):
                        pe.wait_ge(out_ready, t - 1)
                    conv(c2_ps, conv2, c1[1 - b], P).then_inc(c2_done, 1)
                pe.wait_ge(relu_act, 2 * t + 2)
                pe.wait_ge(relu_dve, t + 1)
                for k in range(2):
                    for pair in range(ROWS // 2):
                        q = QUAD * pair
                        last = nc.tensor.matmul(upd_ps[q:q + QUAD, :], mix2[:, k, :], hid[:, 2 * pair + k, :],
                                                start=(k == 0), stop=(k == 1))
                last.then_inc(upd_done, 1)

            pe.wait_ge(weights_loaded, 16 * LOADS)
            steps(pe, step)
            pe.wait_ge(x1_ready, STEPS)
            pe.wait_ge(c1_carry, STEPS - 1)
            conv(c1_ps, conv1, x1[1], NEW).then_inc(c1_done, 1)
            pe.wait_ge(c1_main, STEPS)
            pe.wait_ge(out_ready, STEPS - 1)
            conv(c2_ps, conv2, c1[1], P).then_inc(c2_done, 1)

        @block.scalar
        def _(act):
            def c1_of(t, b):
                at = t - 1
                act.wait_ge(c1_done, t)
                if after(t, 1):
                    act.wait_ge(c2_done, t - 1)
                nc.scalar.activation(c1[1 - b][0:NEW, :, 1:1 + W], wide(c1_ps[0:NEW, :]), ACT.Relu,
                                     bias=c1_bias_at[0:NEW, bass.ds(at, 1)],
                                     scale=c1_keep[0:NEW, bass.ds(at, 1)]).then_inc(c1_main, 1)

            def carry_of(t, b):
                at = t - 1
                nc.scalar.activation(c1[b][NEW:P, :, 1:1 + W], wide(c1_ps[NEW - QUAD:NEW, :]), ACT.Relu,
                                     bias=c1_bias_at[NEW - QUAD:NEW, bass.ds(at, 1)],
                                     scale=c1_keep[NEW - QUAD:NEW, bass.ds(at, 1)]).then_inc(c1_carry, 1)

            def relu(t, pair, b):
                act.wait_ge(h_done, 3 * t + pair + 1)
                nc.scalar.activation(hid[:, 2 * pair:2 * pair + 2, :], h_ps[(pair + b) % 2][:], ACT.Relu,
                                     bias=mix1_bias[:, 0:1]).then_inc(relu_act, 1)

            def step(t, b, half):
                act.wait_ge(y_done, t + 1)
                if after(t, 0):
                    act.wait_ge(h_done, 3 * t)
                nc.scalar.copy(stack_a[0:64, :], y_ps[0:64, :]).then_inc(y_hi, 1)
                nc.scalar.copy(stack_b[64:96, :], y_ps[64:96, :]).then_inc(y_hi, 1)
                act.wait_ge(x_loaded[b], half * 32 + 32)
                if after(t, 0):
                    act.wait_ge(x1_ready, t)
                nc.scalar.activation(x_b[b][:], x_in[b][0:NEW, :, 1:1 + W], ACT.Identity,
                                     bias=x1_bias_at[0:NEW, bass.ds(t, 1)]).then_inc(xb_ready, 1)
                if after(t, 0):
                    c1_of(t, b)
                if after(t, 0):
                    act.wait_ge(upd_done, t)
                relu(t, 0, b)
                if after(t, 0):
                    carry_of(t, b)
                relu(t, 2, b)

            act.wait_ge(cleared, 6)
            act.wait_ge(tables_ready, 2)
            steps(act, step)
            c1_of(STEPS, 0)

        @block.vector
        def _(dve):
            def out_of(t, b, half_before):
                dve.wait_ge(c2_done, t)
                if after(t, 2):
                    dve.wait_ge(stored[1 - b], half_before * 32)
                nc.vector.scalar_tensor_tensor(out_sb[1 - b][:], wide(c2_ps[:]), out_bias[:, 0:1],
                                               x1[1 - b][:, :, 1:1 + W], ALU.add, ALU.add
                                               ).then_inc(out_ready, 1)

            def step(t, b, half):
                dve.wait_ge(y_hi, 2 * t + 2)
                nc.vector.tensor_tensor(stack_a[64:128, :], y_ps[0:64, :], stack_a[0:64, :].bitcast(f32),
                                        ALU.subtract)
                nc.vector.tensor_tensor(stack_b[96:128, :], y_ps[64:96, :], stack_b[64:96, :].bitcast(f32),
                                        ALU.subtract).then_inc(y_lo, 1)
                dve.wait_ge(h_done, 3 * t + 2)
                if after(t, 0):
                    dve.wait_ge(upd_done, t)
                nc.vector.tensor_scalar(hid[:, 2:4, :], h_ps[(1 + b) % 2][:], mix1_bias[:, 0:1], 0.0,
                                        ALU.add, ALU.max).then_inc(relu_dve, 1)
                if after(t, 0):
                    out_of(t, b, half if b else half - 1)
                dve.wait_ge(upd_done, t + 1)
                dve.wait_ge(xb_ready, t + 1)
                if after(t, 0):
                    dve.wait_ge(c1_done, t)
                    dve.wait_ge(out_ready, t)
                nc.vector.scalar_tensor_tensor(x1[b][0:NEW, :, 1:1 + W], wide(upd_ps[0:NEW, :]),
                                               x1_keep[0:NEW, bass.ds(t, 1)], x_b[b][:],
                                               ALU.mult, ALU.add)
                nc.vector.scalar_tensor_tensor(x1[1 - b][NEW:P, :, 1:1 + W], wide(upd_ps[NEW - QUAD:NEW, :]),
                                               x1_keep[NEW - QUAD:NEW, bass.ds(t, 1)], x_b[b][NEW - QUAD:NEW],
                                               ALU.mult, ALU.add).then_inc(x1_ready, 1)

            dve.wait_ge(weights_loaded, 16 * LOADS)
            nc.vector.tensor_copy(mix1_hi[:], mix1_raw[:]).then_inc(mix1_split, 1)
            dve.wait_ge(mix1_split, 1)
            nc.vector.tensor_tensor(mix1_lo[:], mix1_raw[:], mix1_hi[:].bitcast(f32),
                                    ALU.subtract).then_inc(mix1_split, 1)
            nc.vector.tensor_scalar(x1_bias_at[:], x1_keep[:], x1_bias[:, 0:1], None, ALU.mult
                                    ).then_inc(tables_ready, 1)
            nc.vector.tensor_scalar(c1_bias_at[:], c1_keep[:], c1_bias[:, 0:1], None, ALU.mult
                                    ).then_inc(tables_ready, 1)
            steps(dve, step)
            out_of(STEPS, 0, STEPS // 2 - 1)


def wide(ap):
    return ap.rearrange("p (s w) -> p s w", s=SIDE)


def banded(w, rows_in, rows_out, places):
    m = np.zeros((P, TAPS, places * CH), w.dtype)
    for i, ri in enumerate(rows_in):
        for o, ro in rows_out.items():
            if 0 <= ri - ro + 1 < 3:
                m[i * CH:(i + 1) * CH, :, o * CH:(o + 1) * CH] = w[:, :, ri - ro + 1, :].transpose(1, 2, 0)
    return m


def kernel(x, L0_conv_conv_w, L0_conv_w1, L0_conv_b1, L0_conv_w2, L0_conv_b2,
           L1_conv_w1, L1_conv_b1, L1_conv_w2, L1_conv_b2):
    import concourse.bacc as bacc
    from concourse.bass_utils import run_bass_kernel_spmd
    f = np.float32
    x, cw, w1, b1, w2, b2, d1, e1, d2, e2 = (np.asarray(a) for a in (
        x, L0_conv_conv_w, L0_conv_w1, L0_conv_b1, L0_conv_w2, L0_conv_b2,
        L1_conv_w1, L1_conv_b1, L1_conv_w2, L1_conv_b2))

    tall = np.zeros((1 + PAIRS * PITCH + 8, CH, SIDE, WP), f)
    body = tall[1:1 + PAIRS * PITCH].reshape(PAIRS, PITCH, CH, SIDE, WP)
    body[:, :H, :, :, 1:1 + W] = x.reshape(PAIRS, SIDE, CH, H, W).transpose(0, 3, 2, 1, 4)

    w1t = w1.T
    mix1 = np.zeros((P, ROWS, HID), f)
    for r in range(ROWS):
        for at in ((r * CH, 64 + r * CH) if r < STACKED else (r * CH, QUAD + r * CH)):
            mix1[at:at + CH, r] = w1t
    mix2 = np.zeros((P, 2, QUAD), f)
    for k in range(2):
        mix2[:, k, k * CH:(k + 1) * CH] = w2.T

    inside = np.arange(STEPS * ROWS).reshape(STEPS, ROWS) % PITCH
    x1_mask = np.zeros((P, STEPS), f)
    x1_mask[:NEW] = np.repeat((inside < H).T, CH, 0)
    inside = (np.arange(STEPS * ROWS).reshape(STEPS, ROWS) - 1) % PITCH
    c1_mask = np.zeros((P, STEPS), f)
    c1_mask[:NEW] = np.repeat((inside < H).T, CH, 0)

    arrays = {
        "xt": tall.reshape(-1, SIDE * WP),
        "conv0_w": banded(cw, (0, 1, 2, 3, 4, 5, -1, 6), {i: i for i in range(ROWS)}, ROWS),
        "conv1_w": banded(d1, (0, 1, 2, 3, 4, 5, -2, -1), {i: i - 1 for i in range(ROWS)}, ROWS),
        "conv2_w": banded(d2, (-1, 0, 1, 2, 3, 4, -3, -2), {0: 0, 1: 1, 2: 2, 3: 3, 6: -2, 7: -1}, 8),
        "mix1_w": mix1, "mix2_w": mix2,
        "mix1_b": b1.reshape(P, 1),
        "x1_b": np.tile(b2, 8).reshape(P, 1), "c1_b": np.tile(e1, 8).reshape(P, 1),
        "out_b": np.tile(e2, 8).reshape(P, 1),
        "x1_mask": x1_mask, "c1_mask": c1_mask,
    }
    nc = bacc.Bacc("TRN2", target_bir_lowering=False, num_devices=1)
    args = {}
    for name, a in arrays.items():
        arrays[name] = a = np.ascontiguousarray(a)
        args[name] = nc.dram_tensor(name, a.shape, mybir.dt.from_np(a.dtype), kind="ExternalInput").ap()
    out = nc.dram_tensor("out", (STEPS * NEW, SIDE * W), mybir.dt.float32, kind="ExternalOutput").ap()
    build_program(nc, out=out, **args)
    r = run_bass_kernel_spmd(nc, [arrays], core_ids=[0])
    got = np.asarray(r.results[0]["out"]).reshape(STEPS * ROWS, CH, SIDE, W)
    got = got.reshape(PAIRS, PITCH, CH, SIDE, W)[:, 2:].transpose(0, 3, 2, 1, 4)
    return np.ascontiguousarray(got).reshape(IMAGES, CH, H, W)
```

```python
import numpy as np
import concourse.bass as bass
import concourse.mybir as mybir
from contextlib import ExitStack

IMAGES, CH, H, W = 32, 16, 256, 256
HID = 128
SIDE = 2
COLS = SIDE * W
PAIRS = IMAGES // SIDE
ROWS = 6
PITCH = H + 2
BLOCKS = PAIRS * PITCH // ROWS
WP = W + 2
QUAD = 32
P = 128
TAPS = 3
NEW = ROWS * CH
DUOS = ROWS // 2
Y_AT = (64, 96, 0)
LAG = 4
RING = 4
PEELED = 2 * RING
assert PITCH % ROWS == 0 and BLOCKS % RING == 0


def build_program(nc, xt, conv0_w, conv1_w, conv2_w, mix1_w, mix2_w, mix1_b, x1_b, c1_b, out_b,
                  x1_mask, c1_mask, out):
    f32, f32r = mybir.dt.float32, mybir.dt.float32r
    ALU, ACT = mybir.AluOpType, mybir.ActivationFunctionType
    with ExitStack() as ctx:
        def sbuf(name, shape, dt=f32):
            return ctx.enter_context(nc.sbuf_tensor(name, shape, dt))

        def psum(name, shape):
            return ctx.enter_context(nc.psum_tensor(name, shape, f32))

        def sem(name):
            return ctx.enter_context(nc.semaphore(name))

        conv0 = sbuf("conv0", [P, 2, P])
        conv1 = sbuf("conv1", [P, TAPS, P])
        conv2 = sbuf("conv2", [P, TAPS, P])
        mix1_raw = sbuf("mix1_raw", [P, 2, HID])
        mix1_hi = sbuf("mix1_hi", [P, 2, HID], f32r)
        mix1 = sbuf("mix1", [P, 2, HID], f32r)
        mix2 = sbuf("mix2", [P, 2, QUAD])
        mix1_bias = sbuf("mix1_bias", [P, 1])
        x1_bias = sbuf("x1_bias", [P, 1])
        c1_bias = sbuf("c1_bias", [P, 1])
        out_bias = sbuf("out_bias", [P, 1])
        x1_keep = sbuf("x1_keep", [P, BLOCKS])
        c1_keep = sbuf("c1_keep", [P, BLOCKS])
        x1_bias_at = sbuf("x1_bias_at", [P, BLOCKS])
        c1_bias_at = sbuf("c1_bias_at", [P, BLOCKS])

        x_in = [sbuf(f"x_in{i}", [P, DUOS, SIDE * WP]) for i in range(RING)]
        x_mid = [sbuf(f"x_mid{i}", [NEW, SIDE, WP]) for i in range(RING)]
        x_b = [sbuf(f"x_b{i}", [NEW, SIDE, W]) for i in range(2)]
        y_parts = [sbuf(f"y_parts{i}", [P, DUOS, COLS], f32r) for i in range(2)]
        hid = [sbuf(f"hid{i}", [P, ROWS, COLS]) for i in range(2)]
        x1 = [sbuf(f"x1_{i}", [P, SIDE, WP]) for i in range(RING)]
        c1 = [sbuf(f"c1_{i}", [P, SIDE, WP]) for i in range(2)]
        out_sb = [sbuf(f"out_sb{i}", [P, SIDE, W]) for i in range(2)]

        y_ps = psum("y_ps", [P, COLS])
        h_ps = [psum(f"h_ps{i}", [P, 2, COLS]) for i in range(2)]
        upd_ps = psum("upd_ps", [P, COLS])
        c1_ps = psum("c1_ps", [P, COLS])
        c2_ps = psum("c2_ps", [P, COLS])

        weights_loaded = sem("weights_loaded")
        x_loaded = [sem(f"x_loaded{i}") for i in range(RING)]
        x_doubled = [sem(f"x_doubled{i}") for i in range(RING)]
        mid_loaded = [sem(f"mid_loaded{i}") for i in range(RING)]
        y_doubled = [sem(f"y_doubled{i}") for i in range(2)]
        stored = [sem(f"stored{i}") for i in range(2)]
        cleared = sem("cleared")
        unused_set = sem("unused_set")
        mix1_split = sem("mix1_split")
        tables_ready = sem("tables_ready")
        y_done = sem("y_done")
        y_hi = sem("y_hi")
        y_lo = sem("y_lo")
        h_done = sem("h_done")
        relu_act = sem("relu_act")
        relu_dve = sem("relu_dve")
        upd_done = sem("upd_done")
        xb_ready = sem("xb_ready")
        x1_ready = sem("x1_ready")
        c1_done = sem("c1_done")
        c1_new = sem("c1_new")
        c1_ready = sem("c1_ready")
        c2_done = sem("c2_done")
        out_ready = sem("out_ready")

        LOADS = 11
        block = ctx.enter_context(nc.Block())

        def exists(n):
            return not isinstance(n, int) or 0 <= n < BLOCKS

        def uses(rnd, k, m):
            return RING // m * rnd + k // m

        def steps(engine, step):
            for k in range(PEELED):
                step(0, k)
            with engine.Fori(PEELED // RING, BLOCKS // RING - 1) as rnd:
                for k in range(RING):
                    step(rnd, k)
            for k in range(BLOCKS - RING, BLOCKS + LAG):
                step(0, k)

        @block.sync
        def _(sp):
            def load_x(n, b):
                first = n * NEW
                for to, rows, at in ((0, 2, 1), (QUAD, 1, 0), (QUAD + CH, 1, 3)):
                    src = xt[bass.ds(first + at * CH, NEW), :].rearrange("(d q) w -> q d w", d=DUOS)
                    sp.dma_start(x_in[b][to:to + rows * CH], src[0:rows * CH]).then_inc(x_loaded[b], 16)
                sp.dma_start(x_mid[b][:].rearrange("p s w -> p (s w)"),
                             xt[bass.ds(first + CH, NEW), :]).then_inc(mid_loaded[b], 16)

            def double_x(b, use):
                sp.wait_ge(x_loaded[b], 48 * use + 48)
                sp.dma_start(x_in[b][64:P, :, 0:SIDE * WP - 1],
                             x_in[b][0:64, :, 1:SIDE * WP]).then_inc(x_doubled[b], 16)

            def step(rnd, k):
                t = RING * rnd + k
                if exists(t + 1):
                    double_x((k + 1) % RING, uses(rnd, k + 1, RING))
                if exists(t):
                    sp.wait_ge(y_lo, DUOS * (t + 1))
                    sp.dma_start(y_parts[k % 2][64:P].bitcast(f32),
                                 y_parts[k % 2][0:64].bitcast(f32)).then_inc(y_doubled[k % 2], 16)
                if exists(t + 2) and exists(t - 2):
                    sp.wait_ge(xb_ready, t - 1)
                    load_x(t + 2, (k + 2) % RING)
                if exists(t - LAG):
                    sp.wait_ge(out_ready, t - LAG + 1)
                    first, b = (t - LAG) * NEW, k % 2
                    sp.dma_start(out[bass.ds(first, QUAD), :],
                                 out_sb[b][NEW:P].rearrange("p s w -> p (s w)")).then_inc(stored[b], 16)
                    sp.dma_start(out[bass.ds(first + QUAD, NEW - QUAD), :],
                                 out_sb[b][0:NEW - QUAD].rearrange("p s w -> p (s w)")).then_inc(stored[b], 16)

            load_x(0, 0)
            for dst, src in ((conv0, conv0_w), (mix1_raw, mix1_w), (conv1, conv1_w), (conv2, conv2_w),
                             (mix2, mix2_w), (mix1_bias, mix1_b), (x1_bias, x1_b), (c1_bias, c1_b),
                             (out_bias, out_b), (x1_keep, x1_mask), (c1_keep, c1_mask)):
                sp.dma_start(dst[:], src).then_inc(weights_loaded, 16)
            double_x(0, 0)
            for n in range(1, RING):
                load_x(n, n)
            steps(sp, step)
            for b in range(2):
                sp.wait_ge(stored[b], 32 * (BLOCKS // 2))

        @block.gpsimd
        def _(pool):
            for tile in (*x1, *c1):
                nc.gpsimd.memset(tile[:], 0.0).then_inc(cleared, 1)

        @block.tensor
        def _(pe):
            def step(rnd, k):
                t = RING * rnd + k
                n_y, n_h, n_upd, n_c1, n_c2 = t, t - 1, t - 2, t - 3, t - 4

                def product(ps, q, weights, src, tap):
                    rows = slice(QUAD * q, QUAD * (q + 1))
                    return nc.tensor.matmul(ps[rows, :], weights[:, tap, rows], src[:, :, tap:tap + W],
                                            start=(tap == 0), stop=(tap == TAPS - 1))

                def y(q, part):
                    if exists(n_y):
                        rows, duo = slice(QUAD * q, QUAD * (q + 1)), Y_AT.index(QUAD * q)
                        src = x_in[k % RING][:, duo, :].rearrange("p (s w) -> p s w", s=SIDE)
                        return nc.tensor.matmul(y_ps[rows, :], conv0[:, part, rows], src[:, :, part:part + W],
                                                start=(part == 0), stop=(part == 1))

                def upd(q, row):
                    if exists(n_upd):
                        return nc.tensor.matmul(upd_ps[QUAD * q:QUAD * (q + 1), :], mix2[:, row, :],
                                                hid[k % 2][:, 2 * q + row, :], start=(row == 0), stop=(row == 1))

                def c1_(q, tap):
                    if exists(n_c1):
                        return product(c1_ps, q, conv1, x1[(k - 3) % RING], tap)

                def c2_(q, tap):
                    if exists(n_c2):
                        return product(c2_ps, q, conv2, c1[k % 2], tap)

                def hidden(duo):
                    if exists(n_h):
                        for row in range(2):
                            last = nc.tensor.matmul(h_ps[(duo + k - 1) % 2][:, row, :], mix1[:, row, :],
                                                    y_parts[(k - 1) % 2][:, duo, :], start=True, stop=True)
                        last.then_inc(h_done, 1)

                if exists(n_y):
                    pe.wait_ge(x_doubled[k % RING], 16 * uses(rnd, k, RING) + 16)
                    if exists(n_y - 1):
                        pe.wait_ge(y_lo, DUOS * n_y)
                if exists(n_upd):
                    pe.wait_ge(relu_act, 2 * (n_upd + 1))
                    pe.wait_ge(relu_dve, n_upd + 1)
                    if exists(n_upd - 1):
                        pe.wait_ge(x1_ready, n_upd)
                y(0, 0), upd(1, 0), y(2, 0), y(3, 0)
                y(0, 1), upd(1, 1), y(2, 1)
                if exists(n_y):
                    y(3, 1).then_inc(y_done, 1)
                if exists(n_h):
                    pe.wait_ge(y_doubled[(k - 1) % 2], 16 * uses(rnd, k - 1, 2) + 16)
                    if exists(n_h - 1):
                        pe.wait_ge(relu_act, 2 * n_h)
                hidden(0)
                hidden(1)
                if exists(n_c1):
                    pe.wait_ge(x1_ready, n_c1 + 1)
                    if exists(n_c1 - 1):
                        pe.wait_ge(c1_new, n_c1)
                upd(0, 0), c1_(1, 0), upd(2, 0), c1_(3, 0)
                upd(0, 1), c1_(1, 1)
                if exists(n_upd):
                    upd(2, 1).then_inc(upd_done, 1)
                c1_(3, 1)
                if exists(n_c2):
                    pe.wait_ge(c1_ready, n_c2 + 1)
                    if exists(n_c2 - 1):
                        pe.wait_ge(out_ready, n_c2)
                c2_(0, 0), c1_(1, 2), c1_(2, 0), c1_(3, 2)
                if exists(n_h):
                    pe.wait_ge(relu_dve, n_h + 1)
                hidden(2)
                c2_(0, 1), c2_(1, 0), c1_(2, 1), c2_(3, 0)
                c2_(0, 2), c2_(1, 1)
                if exists(n_c1):
                    c1_(2, 2).then_inc(c1_done, 1)
                c2_(3, 1)
                c2_(1, 2)
                if exists(n_c2):
                    c2_(3, 2).then_inc(c2_done, 1)

            pe.wait_ge(weights_loaded, 16 * LOADS)
            pe.wait_ge(mix1_split, 3)
            pe.wait_ge(unused_set, 2)
            steps(pe, step)

        @block.scalar
        def _(act):
            def relu_hidden(n, b, duo, bank):
                act.wait_ge(h_done, DUOS * n + duo + 1)
                nc.scalar.activation(hid[b][:, 2 * duo:2 * duo + 2, :], h_ps[bank][:], ACT.Relu,
                                     bias=mix1_bias[:, 0:1]).then_inc(relu_act, 1)

            def step(rnd, k):
                t = RING * rnd + k
                if exists(t):
                    act.wait_ge(y_done, t + 1)
                    if exists(t - 2):
                        act.wait_ge(h_done, DUOS * (t - 1))
                    for duo, at in enumerate(Y_AT):
                        nc.scalar.copy(y_parts[k % 2][0:QUAD, duo, :], y_ps[at:at + QUAD, :]).then_inc(y_hi, 1)
                n = t - 1
                if exists(n):
                    if exists(n - 2):
                        act.wait_ge(upd_done, n - 1)
                    relu_hidden(n, (k - 1) % 2, 1, k % 2)
                n = t - 2
                if exists(n):
                    act.wait_ge(mid_loaded[(k - 2) % RING], 16 * uses(rnd, k - 2, RING) + 16)
                    if exists(n - 2):
                        act.wait_ge(x1_ready, n - 1)
                    nc.scalar.activation(x_b[k % 2][:], x_mid[(k - 2) % RING][:, :, 1:1 + W], ACT.Identity,
                                         bias=x1_bias_at[0:NEW, bass.ds(n, 1)]).then_inc(xb_ready, 1)
                n = t - 1
                if exists(n):
                    relu_hidden(n, (k - 1) % 2, 2, (k - 1) % 2)
                n = t - 3
                if exists(n):
                    act.wait_ge(c1_done, n + 1)
                    if exists(n - 2):
                        act.wait_ge(c2_done, n - 1)
                    nc.scalar.activation(c1[(k - 3) % 2][:, :, 1:1 + W], wide(c1_ps[:]), ACT.Relu,
                                         bias=c1_bias_at[:, bass.ds(n, 1)],
                                         scale=c1_keep[:, bass.ds(n, 1)]).then_inc(c1_new, 1)
                    act.wait_ge(c1_new, n + 1)
                    nc.scalar.copy(c1[(k - 3) % 2][0:QUAD, :, 1:1 + W],
                                   c1[(k - 4) % 2][NEW:P, :, 1:1 + W]).then_inc(c1_ready, 1)

            act.wait_ge(cleared, RING + 2)
            act.wait_ge(unused_set, 2)
            act.wait_ge(tables_ready, 2)
            steps(act, step)

        @block.vector
        def _(dve):
            def step(rnd, k):
                t = RING * rnd + k
                n = t - 1
                if exists(n):
                    dve.wait_ge(h_done, DUOS * n + 1)
                    if exists(n - 2):
                        dve.wait_ge(upd_done, n - 1)
                    nc.vector.tensor_scalar(hid[(k - 1) % 2][:, 0:2, :], h_ps[(k - 1) % 2][:], mix1_bias[:, 0:1], 0.0,
                                            ALU.add, ALU.max).then_inc(relu_dve, 1)
                if exists(t):
                    for duo, at in enumerate(Y_AT):
                        dve.wait_ge(y_hi, DUOS * t + duo + 1)
                        nc.vector.tensor_tensor(y_parts[k % 2][QUAD:64, duo, :], y_ps[at:at + QUAD, :],
                                                y_parts[k % 2][0:QUAD, duo, :].bitcast(f32),
                                                ALU.subtract).then_inc(y_lo, 1)
                n = t - 2
                if exists(n):
                    dve.wait_ge(upd_done, n + 1)
                    dve.wait_ge(xb_ready, n + 1)
                    if exists(n + 1 - RING):
                        dve.wait_ge(out_ready, n + 2 - RING)
                    b, after = (k - 2) % RING, (k - 1) % RING
                    nc.vector.scalar_tensor_tensor(x1[b][0:NEW, :, 1:1 + W], wide(upd_ps[0:NEW, :]),
                                                   x1_keep[0:NEW, bass.ds(n, 1)], x_b[k % 2][:],
                                                   ALU.mult, ALU.add)
                    nc.vector.scalar_tensor_tensor(x1[after][NEW:P, :, 1:1 + W], wide(upd_ps[64:NEW, :]),
                                                   x1_keep[64:NEW, bass.ds(n, 1)], x_b[k % 2][64:NEW],
                                                   ALU.mult, ALU.add).then_inc(x1_ready, 1)
                n = t - 4
                if exists(n):
                    dve.wait_ge(c2_done, n + 1)
                    if exists(n - 2):
                        dve.wait_ge(stored[k % 2], 32 * uses(rnd, k - 4, 2))
                    nc.vector.scalar_tensor_tensor(out_sb[k % 2][:], wide(c2_ps[:]), out_bias[:, 0:1],
                                                   x1[(k - 4) % RING][:, :, 1:1 + W],
                                                   ALU.add, ALU.add).then_inc(out_ready, 1)

            nc.vector.memset(c1_ps[0:QUAD, :], 0.0).then_inc(unused_set, 1)
            nc.vector.memset(c2_ps[64:NEW, :], 0.0).then_inc(unused_set, 1)
            dve.wait_ge(weights_loaded, 16 * LOADS)
            nc.vector.tensor_copy(mix1_hi[:], mix1_raw[:]).then_inc(mix1_split, 1)
            dve.wait_ge(mix1_split, 1)
            nc.vector.tensor_copy(mix1[0:64], mix1_hi[0:64].bitcast(f32)).then_inc(mix1_split, 1)
            nc.vector.tensor_tensor(mix1[64:P], mix1_raw[64:P], mix1_hi[64:P].bitcast(f32),
                                    ALU.subtract).then_inc(mix1_split, 1)
            nc.vector.tensor_scalar(x1_bias_at[:], x1_keep[:], x1_bias[:, 0:1], None, ALU.mult
                                    ).then_inc(tables_ready, 1)
            nc.vector.tensor_scalar(c1_bias_at[:], c1_keep[:], c1_bias[:, 0:1], None, ALU.mult
                                    ).then_inc(tables_ready, 1)
            dve.wait_ge(cleared, RING + 2)
            steps(dve, step)


def wide(ap):
    return ap.rearrange("p (s w) -> p s w", s=SIDE)


def banded(w, rows_in, rows_out):
    m = np.zeros((P, TAPS, P), w.dtype)
    for i, ri in enumerate(rows_in):
        for o, ro in enumerate(rows_out):
            if ro is not None and 0 <= ri - ro + 1 < TAPS:
                m[i * CH:(i + 1) * CH, :, o * CH:(o + 1) * CH] = w[:, :, ri - ro + 1, :].transpose(1, 2, 0)
    return m


def kernel(x, L0_conv_conv_w, L0_conv_w1, L0_conv_b1, L0_conv_w2, L0_conv_b2,
           L1_conv_w1, L1_conv_b1, L1_conv_w2, L1_conv_b2):
    import concourse.bacc as bacc
    from concourse.bass_utils import run_bass_kernel_spmd
    f = np.float32
    x, cw, w1, b1, w2, b2, d1, e1, d2, e2 = (np.asarray(a) for a in (
        x, L0_conv_conv_w, L0_conv_w1, L0_conv_b1, L0_conv_w2, L0_conv_b2,
        L1_conv_w1, L1_conv_b1, L1_conv_w2, L1_conv_b2))

    tall = np.zeros((1 + PAIRS * PITCH + 8, CH, SIDE, WP), f)
    body = tall[1:1 + PAIRS * PITCH].reshape(PAIRS, PITCH, CH, SIDE, WP)
    body[:, :H, :, :, 1:1 + W] = x.reshape(PAIRS, SIDE, CH, H, W).transpose(0, 3, 2, 1, 4)

    mix1 = np.zeros((P, 2, HID), f)
    for at in range(0, P, QUAD):
        for k in range(2):
            mix1[at + k * CH:at + (k + 1) * CH, k] = w1.T
    bands = banded(cw, (0, 1, -1, 2), (0, 1) * 4)
    conv0 = np.zeros((P, 2, P), f)
    conv0[0:64, 0], conv0[64:P, 0], conv0[64:P, 1] = bands[0:64, 0], bands[0:64, 1], bands[0:64, 2]
    mix2 = np.zeros((P, 2, QUAD), f)
    for k in range(2):
        mix2[:, k, k * CH:(k + 1) * CH] = w2.T

    inside = np.arange(BLOCKS * ROWS).reshape(BLOCKS, ROWS) % PITCH
    x1_mask = np.zeros((P, BLOCKS), f)
    x1_mask[:NEW] = np.repeat((inside < H).T, CH, 0)
    inside = (np.arange(BLOCKS * ROWS).reshape(BLOCKS, ROWS) - 1) % PITCH
    c1_mask = np.zeros((P, BLOCKS), f)
    c1_mask[QUAD:] = np.repeat((inside < H).T, CH, 0)

    arrays = {
        "xt": tall.reshape(-1, SIDE * WP),
        "conv0_w": conv0,
        "conv1_w": banded(d1, (0, 1, 2, 3, 4, 5, -2, -1), (None, None, -1, 0, 1, 2, 3, 4)),
        "conv2_w": banded(d2, (-3, -2, -1, 0, 1, 2, 3, 4), (0, 1, 2, 3, None, None, -2, -1)),
        "mix1_w": mix1, "mix2_w": mix2,
        "mix1_b": b1.reshape(P, 1),
        "x1_b": np.tile(b2, 8).reshape(P, 1), "c1_b": np.tile(e1, 8).reshape(P, 1),
        "out_b": np.tile(e2, 8).reshape(P, 1),
        "x1_mask": x1_mask, "c1_mask": c1_mask,
    }
    nc = bacc.Bacc("TRN2", target_bir_lowering=False, num_devices=1)
    args = {}
    for name, a in arrays.items():
        arrays[name] = a = np.ascontiguousarray(a)
        args[name] = nc.dram_tensor(name, a.shape, mybir.dt.from_np(a.dtype), kind="ExternalInput").ap()
    out = nc.dram_tensor("out", (BLOCKS * NEW, COLS), mybir.dt.float32, kind="ExternalOutput").ap()
    build_program(nc, out=out, **args)
    r = run_bass_kernel_spmd(nc, [arrays], core_ids=[0])
    got = np.asarray(r.results[0]["out"]).reshape(BLOCKS * ROWS, CH, SIDE, W)
    got = got.reshape(PAIRS, PITCH, CH, SIDE, W)[:, 2:].transpose(0, 3, 2, 1, 4)
    return np.ascontiguousarray(got).reshape(IMAGES, CH, H, W)
```

```python
import numpy as np
import concourse.bass as bass
import concourse.mybir as mybir
from contextlib import ExitStack

IMAGES, CH, H, W = 32, 16, 256, 256
HIDDEN = 128
SIDE = 2
COLS = SIDE * W
PAIRS = IMAGES // SIDE
ROWS = 6
PITCH = H + 2
BLOCKS = PAIRS * PITCH // ROWS
WP = W + 2
QUAD = 32
P = 128
SHIFTED = 3 * QUAD
TAPS = 3
NEW = ROWS * CH
DUOS = ROWS // 2
Y_AT = (64, 96, 0)
UPD_AT = (0, 32, 96)
C1_AT = (32, 64, 96)
C2_AT = (0, 32, 64)
HID, UPD, CONV1, CONV2 = 2, 3, 5, 7
X1, C1, OUT = UPD + 1, CONV1 + 1, CONV2 + 1
RING = 4
BEFORE = 2 * CH
PEELED = 3 * RING
assert PITCH % ROWS == 0 and BLOCKS % RING == 0


def build_program(nc, xt, conv0_w, conv1_w, conv2_w, mix1_w, mix2_w, mix1_b, x1_b, c1_b, out_b,
                  x1_mask, c1_mask, out):
    f32, f32r = mybir.dt.float32, mybir.dt.float32r
    ALU, ACT = mybir.AluOpType, mybir.ActivationFunctionType
    with ExitStack() as ctx:
        def sbuf(name, shape, dt=f32):
            return ctx.enter_context(nc.sbuf_tensor(name, shape, dt))

        def psum(name, shape):
            return ctx.enter_context(nc.psum_tensor(name, shape, f32))

        def sem(name):
            return ctx.enter_context(nc.semaphore(name))

        conv0 = sbuf("conv0", [SHIFTED, 2, QUAD])
        conv1 = sbuf("conv1", [SHIFTED, 2, QUAD])
        conv2 = sbuf("conv2", [P, 2, QUAD])
        mix1_raw = sbuf("mix1_raw", [P, 2, HIDDEN])
        mix1_hi = sbuf("mix1_hi", [P, 2, HIDDEN], f32r)
        mix1 = sbuf("mix1", [P, 2, HIDDEN], f32r)
        mix2 = sbuf("mix2", [P, 2, QUAD])
        mix1_bias = sbuf("mix1_bias", [P, 1])
        x1_bias = sbuf("x1_bias", [P, 1])
        c1_bias = sbuf("c1_bias", [P, 1])
        out_bias = sbuf("out_bias", [P, 1])
        x1_keep = sbuf("x1_keep", [P, BLOCKS])
        c1_keep = sbuf("c1_keep", [P, BLOCKS])
        x1_bias_at = sbuf("x1_bias_at", [P, BLOCKS])
        c1_bias_at = sbuf("c1_bias_at", [P, BLOCKS])

        x_shifts = [sbuf(f"x_shifts{i}", [SHIFTED, DUOS, SIDE * WP]) for i in range(RING)]
        x_mid = [sbuf(f"x_mid{i}", [NEW, SIDE, WP]) for i in range(RING)]
        x_b = [sbuf(f"x_b{i}", [NEW, SIDE, W]) for i in range(2)]
        y_parts = [sbuf(f"y_parts{i}", [P, DUOS, COLS], f32r) for i in range(RING)]
        hid = [sbuf(f"hid{i}", [P, ROWS, COLS]) for i in range(2)]
        x1_shifts = [sbuf(f"x1_shifts{i}", [SHIFTED, DUOS, SIDE * WP]) for i in range(RING)]
        c1_shifts = [sbuf(f"c1_shifts{i}", [P, DUOS, SIDE * WP]) for i in range(RING)]
        out_sb = [sbuf(f"out_sb{i}", [NEW, COLS]) for i in range(2)]

        y_ps = psum("y_ps", [P, COLS])
        h_ps = [psum(f"h_ps{i}", [P, 2, COLS]) for i in range(2)]
        upd_ps = psum("upd_ps", [P, COLS])
        c1_ps = psum("c1_ps", [P, COLS])
        c2_ps = psum("c2_ps", [P, COLS])

        weights_loaded = sem("weights_loaded")
        x_before = sem("x_before")
        x_loaded = [sem(f"x_loaded{i}") for i in range(RING)]
        x_shifted = [sem(f"x_shifted{i}") for i in range(RING)]
        mid_loaded = [sem(f"mid_loaded{i}") for i in range(RING)]
        x1_shifted = [sem(f"x1_shifted{i}") for i in range(RING)]
        c1_shifted = [sem(f"c1_shifted{i}") for i in range(RING)]
        y_doubled = [sem(f"y_doubled{i}") for i in range(RING)]
        stored = [sem(f"stored{i}") for i in range(2)]
        cleared = sem("cleared")
        mix1_split = sem("mix1_split")
        tables_ready = sem("tables_ready")
        y_done = sem("y_done")
        y_hi = sem("y_hi")
        y_lo = sem("y_lo")
        h_done = sem("h_done")
        relu_act = sem("relu_act")
        relu_dve = sem("relu_dve")
        upd_done = sem("upd_done")
        xb_ready = sem("xb_ready")
        x1_ready = sem("x1_ready")
        copy_clear = sem("copy_clear")
        x1_copied = sem("x1_copied")
        c1_done = sem("c1_done")
        c1_ready = sem("c1_ready")
        c2_done = sem("c2_done")
        out_ready = sem("out_ready")

        LOADS = 11
        block = ctx.enter_context(nc.Block())

        def exists(n):
            return not isinstance(n, int) or 0 <= n < BLOCKS

        def uses(rnd, k, m):
            return RING // m * rnd + k // m

        def steps(engine, step):
            for k in range(PEELED):
                step(0, k)
            with engine.Fori(PEELED // RING, BLOCKS // RING - 1) as rnd:
                for k in range(RING):
                    step(rnd, k)
            for k in range(BLOCKS - RING, BLOCKS + OUT):
                step(0, k)

        @block.sync
        def _(sp):
            def load_x(n, b):
                sp.dma_start(x_shifts[b][0:QUAD], xt[bass.ds(n * NEW + BEFORE, NEW), :].rearrange(
                    "(d q) w -> q d w", d=DUOS)).then_inc(x_loaded[b], 16)

            def load_mid(n, b):
                sp.dma_start(x_mid[b][:].rearrange("p s w -> p (s w)"),
                             xt[bass.ds(n * NEW + CH, NEW), :]).then_inc(mid_loaded[b], 16)

            def shift(tile, done):
                for by in range(1, TAPS):
                    sp.dma_start(tile[QUAD * by:QUAD * (by + 1), :, 0:SIDE * WP - 2],
                                 tile[0:QUAD, :, by:by + SIDE * WP - 2]).then_inc(done, 16)

            def shift_x(b, use):
                sp.wait_ge(x_loaded[b], 16 * use + 16)
                shift(x_shifts[b], x_shifted[b])

            def step(rnd, k):
                t = RING * rnd + k
                if exists(t - OUT):
                    sp.wait_ge(out_ready, t - OUT + 1)
                    sp.dma_start(out[bass.ds((t - OUT) * NEW, NEW), :], out_sb[(k - OUT) % 2][:]
                                 ).then_inc(stored[(k - OUT) % 2], 16)
                if exists(t - 1):
                    if exists(t - 5):
                        sp.wait_ge(xb_ready, t - 4)
                    load_mid(t - 1, (k - 1) % RING)
                if exists(t + 2):
                    shift_x((k + 2) % RING, uses(rnd, k + 2, RING))
                if exists(t - X1):
                    sp.wait_ge(x1_ready, DUOS * (t - X1 + 1))
                    shift(x1_shifts[(k - X1) % RING], x1_shifted[(k - X1) % RING])
                if exists(t - C1):
                    sp.wait_ge(c1_ready, DUOS * (t - C1 + 1))
                    shift(c1_shifts[(k - C1) % RING], c1_shifted[(k - C1) % RING])
                if exists(t + 3):
                    sp.wait_ge(y_done, t + 1)
                    load_x(t + 3, (k + 3) % RING)
                if exists(t):
                    sp.wait_ge(y_lo, DUOS * (t + 1))
                    sp.dma_start(y_parts[k % RING][64:P].bitcast(f32),
                                 y_parts[k % RING][0:64].bitcast(f32)).then_inc(y_doubled[k % RING], 16)

            load_x(0, 0)
            for dst, src in ((conv0, conv0_w), (mix1_raw, mix1_w), (conv1, conv1_w), (conv2, conv2_w),
                             (mix2, mix2_w), (mix1_bias, mix1_b), (x1_bias, x1_b), (c1_bias, c1_b),
                             (out_bias, out_b), (x1_keep, x1_mask), (c1_keep, c1_mask)):
                sp.dma_start(dst[:], src).then_inc(weights_loaded, 16)
            for by in range(TAPS):
                sp.dma_start(x_shifts[RING - 1][QUAD * by:QUAD * (by + 1), DUOS - 1, 0:SIDE * WP - 2],
                             xt[0:BEFORE, by:by + SIDE * WP - 2]).then_inc(x_before, 16)
            shift_x(0, 0)
            for n in range(1, RING - 1):
                load_x(n, n)
            shift_x(1, 0)
            steps(sp, step)
            for b in range(2):
                sp.wait_ge(stored[b], 16 * (BLOCKS // 2))

        @block.gpsimd
        def _(pool):
            for tile in (*x1_shifts, *c1_shifts):
                nc.gpsimd.memset(tile[:], 0.0).then_inc(cleared, 1)

            def step(rnd, k):
                n = RING * rnd + k - X1
                if exists(n):
                    pool.wait_ge(x1_ready, DUOS * (n + 1))
                    if exists(n - 3):
                        pool.wait_ge(c2_done, n - 2)
                    pool.sem_inc(copy_clear, 1)
                    b = (k - X1) % RING
                    src = x1_shifts[b][0:QUAD].rearrange("p d (s w) -> p d s w", s=SIDE)
                    dst = c1_shifts[b][SHIFTED:P].rearrange("p d (s w) -> p d s w", s=SIDE)
                    nc.gpsimd.tensor_copy(dst[:, :, :, 0:W], src[:, :, :, 1:1 + W]).then_inc(x1_copied, 1)

            pool.wait_ge(cleared, 2 * RING)
            steps(pool, step)

        @block.tensor
        def _(pe):
            def step(rnd, k):
                t = RING * rnd + k
                n_y, n_h, n_upd, n_c1, n_c2 = t, t - HID, t - UPD, t - CONV1, t - CONV2

                def quadrant(ps, q):
                    return ps[QUAD * q:QUAD * (q + 1), :]

                def from_shifts(ps, q, weights, tiles, duo, part):
                    tile, at = tiles[part], (duo - 1 + part) % DUOS
                    src = tile[:, at, :].rearrange("p (s w) -> p s w", s=SIDE)[:, :, 0:W]
                    return nc.tensor.matmul(quadrant(ps, q), weights[:, part, :], src,
                                            start=(part == 0), stop=(part == 1))

                def around(tiles, b, duo):
                    return tiles[(b - (duo == 0)) % RING], tiles[b % RING]

                def y(q, part):
                    if exists(n_y):
                        duo = Y_AT.index(QUAD * q)
                        return from_shifts(y_ps, q, conv0, around(x_shifts, k, duo), duo, part)

                def c2_(q, part):
                    if exists(n_c2):
                        duo = C2_AT.index(QUAD * q)
                        return from_shifts(c2_ps, q, conv2, around(c1_shifts, k - CONV2, duo), duo, part)

                def upd(q, row):
                    if exists(n_upd):
                        duo = UPD_AT.index(QUAD * q)
                        return nc.tensor.matmul(quadrant(upd_ps, q), mix2[:, row, :],
                                                hid[(k - UPD) % 2][:, 2 * duo + row, :], start=(row == 0), stop=(row == 1))

                def c1_(q, part):
                    if exists(n_c1):
                        duo = C1_AT.index(QUAD * q)
                        return from_shifts(c1_ps, q, conv1, around(x1_shifts, k - CONV1, duo), duo, part)

                def hidden(duo):
                    if exists(n_h):
                        for row in range(2):
                            last = nc.tensor.matmul(h_ps[(duo + k) % 2][:, row, :], mix1[:, row, :],
                                                    y_parts[(k - HID) % RING][:, duo, :], start=True, stop=True)
                        last.then_inc(h_done, 1)

                if exists(n_y):
                    pe.wait_ge(x_shifted[k % RING], 32 * uses(rnd, k, RING) + 32)
                    if exists(n_y - 1):
                        pe.wait_ge(y_lo, DUOS * n_y)
                if exists(n_upd):
                    pe.wait_ge(relu_act, 2 * n_upd + 1)
                    if exists(n_upd - 1):
                        pe.wait_ge(x1_ready, DUOS * (n_upd - 1) + 1)
                y(0, 0), upd(1, 0), y(2, 0), y(3, 0)
                y(0, 1)
                if exists(n_upd):
                    upd(1, 1).then_inc(upd_done, 1)
                y(2, 1)
                if exists(n_y):
                    y(3, 1).then_inc(y_done, 1)

                if exists(n_h):
                    pe.wait_ge(y_doubled[(k - HID) % RING], 16 * uses(rnd, k - HID, RING) + 16)
                    if exists(n_h - 1):
                        pe.wait_ge(relu_act, 2 * n_h)
                hidden(0)
                hidden(1)

                if exists(n_upd):
                    pe.wait_ge(relu_dve, n_upd + 1)
                    pe.wait_ge(relu_act, 2 * (n_upd + 1))
                    if exists(n_upd - 1):
                        pe.wait_ge(x1_ready, DUOS * n_upd)
                if exists(n_c1):
                    pe.wait_ge(x1_shifted[(k - CONV1) % RING], 32 * uses(rnd, k - CONV1, RING) + 32)
                    if exists(n_c1 - 1):
                        pe.wait_ge(c1_ready, DUOS * (n_c1 - 1) + 2)
                upd(0, 0), c1_(1, 0), c1_(2, 0), upd(3, 0)
                upd(0, 1), c1_(1, 1)
                if exists(n_c1):
                    c1_(2, 1).then_inc(c1_done, 1)
                if exists(n_upd):
                    upd(3, 1).then_inc(upd_done, 1)

                if exists(n_c1 - 1) and exists(n_c1):
                    pe.wait_ge(c1_ready, DUOS * n_c1)
                if exists(n_c2):
                    pe.wait_ge(c1_shifted[(k - CONV2) % RING], 32 * uses(rnd, k - CONV2, RING) + 32)
                    pe.wait_ge(x1_copied, n_c2 + 1)
                    if exists(n_c2 - 1):
                        pe.wait_ge(out_ready, n_c2)
                c2_(0, 0), c2_(1, 0), c2_(2, 0), c1_(3, 0)
                if exists(n_h):
                    pe.wait_ge(relu_dve, n_h + 1)
                hidden(2)
                if exists(n_c1):
                    c1_(3, 1).then_inc(c1_done, 1)
                c2_(0, 1), c2_(1, 1)
                if exists(n_c2):
                    c2_(2, 1).then_inc(c2_done, 1)

            pe.wait_ge(weights_loaded, 16 * LOADS)
            pe.wait_ge(mix1_split, 3)
            pe.wait_ge(cleared, 2 * RING)
            pe.wait_ge(x_before, 16 * TAPS)
            steps(pe, step)

        @block.scalar
        def _(act):
            def relu_hidden(n, b, duo, bank):
                act.wait_ge(h_done, DUOS * n + duo + 1)
                nc.scalar.activation(hid[b][:, 2 * duo:2 * duo + 2, :], h_ps[bank][:], ACT.Relu,
                                     bias=mix1_bias[:, 0:1]).then_inc(relu_act, 1)

            def c1_pair(n, b, duo):
                rows = slice(C1_AT[duo], C1_AT[duo] + QUAD)
                nc.scalar.activation(wide(c1_shifts[b][0:QUAD, duo, :])[:, :, 1:1 + W], wide(c1_ps[rows, :]),
                                     ACT.Relu, bias=c1_bias_at[rows, bass.ds(n, 1)],
                                     scale=c1_keep[rows, bass.ds(n, 1)]).then_inc(c1_ready, 1)

            def step(rnd, k):
                t = RING * rnd + k
                if exists(t):
                    act.wait_ge(y_done, t + 1)
                    if exists(t - RING):
                        act.wait_ge(h_done, DUOS * (t - RING + 1))
                    for duo, at in enumerate(Y_AT):
                        nc.scalar.copy(y_parts[k % RING][0:QUAD, duo, :], y_ps[at:at + QUAD, :]).then_inc(y_hi, 1)
                n = t - HID
                if exists(n):
                    if exists(n - 2):
                        act.wait_ge(upd_done, 2 * (n - 1))
                    relu_hidden(n, (k - HID) % 2, 1, (k + 1) % 2)
                n = t - CONV1
                if exists(n):
                    act.wait_ge(c1_done, 2 * n + 1)
                    if exists(n - 3):
                        act.wait_ge(c2_done, n - 2)
                    c1_pair(n, (k - CONV1) % RING, 0)
                    c1_pair(n, (k - CONV1) % RING, 1)
                n = t - HID
                if exists(n):
                    relu_hidden(n, (k - HID) % 2, 2, k % 2)
                    act.wait_ge(mid_loaded[(k - HID) % RING], 16 * uses(rnd, k - HID, RING) + 16)
                    if exists(n - 2):
                        act.wait_ge(x1_ready, DUOS * (n - 1))
                    nc.scalar.activation(x_b[(k - HID) % 2][:], x_mid[(k - HID) % RING][:, :, 1:1 + W], ACT.Identity,
                                         bias=x1_bias_at[0:NEW, bass.ds(n, 1)]).then_inc(xb_ready, 1)
                n = t - CONV1
                if exists(n):
                    act.wait_ge(c1_done, 2 * n + 2)
                    c1_pair(n, (k - CONV1) % RING, 2)

            act.wait_ge(cleared, 2 * RING)
            act.wait_ge(tables_ready, 2)
            steps(act, step)

        @block.vector
        def _(dve):
            def step(rnd, k):
                t = RING * rnd + k
                n = t - HID
                if exists(n):
                    dve.wait_ge(h_done, DUOS * n + 1)
                    if exists(n - 2):
                        dve.wait_ge(upd_done, 2 * (n - 1))
                    nc.vector.tensor_scalar(hid[(k - HID) % 2][:, 0:2, :], h_ps[k % 2][:], mix1_bias[:, 0:1], 0.0,
                                            ALU.add, ALU.max).then_inc(relu_dve, 1)
                if exists(t):
                    for duo, at in enumerate(Y_AT):
                        dve.wait_ge(y_hi, DUOS * t + duo + 1)
                        nc.vector.tensor_tensor(y_parts[k % RING][QUAD:64, duo, :], y_ps[at:at + QUAD, :],
                                                y_parts[k % RING][0:QUAD, duo, :].bitcast(f32),
                                                ALU.subtract).then_inc(y_lo, 1)
                n = t - UPD
                if exists(n):
                    dve.wait_ge(xb_ready, n + 1)
                    if exists(n - RING + 1):
                        dve.wait_ge(c1_done, 2 * (n - RING + 2))
                    if exists(n - RING):
                        dve.wait_ge(x1_copied, n - RING + 1)
                    for duo, done in ((1, 1), (0, 2), (2, 2)):
                        dve.wait_ge(upd_done, 2 * n + done)
                        at, to = slice(UPD_AT[duo], UPD_AT[duo] + QUAD), slice(QUAD * duo, QUAD * (duo + 1))
                        dst = wide(x1_shifts[(k - UPD) % RING][0:QUAD, duo, :])
                        nc.vector.scalar_tensor_tensor(dst[:, :, 1:1 + W], wide(upd_ps[at, :]),
                                                       x1_keep[to, bass.ds(n, 1)], x_b[(k - UPD) % 2][to],
                                                       ALU.mult, ALU.add).then_inc(x1_ready, 1)
                n = t - CONV2
                if exists(n):
                    dve.wait_ge(c2_done, n + 1)
                    if exists(n - 2):
                        dve.wait_ge(stored[(k - CONV2) % 2], 16 * uses(rnd, k - CONV2, 2))
                    nc.vector.tensor_scalar(out_sb[(k - CONV2) % 2][:], c2_ps[0:NEW, :], out_bias[0:NEW, 0:1], None,
                                            ALU.add).then_inc(out_ready, 1)

            dve.wait_ge(weights_loaded, 16 * LOADS)
            nc.vector.tensor_copy(mix1_hi[:], mix1_raw[:]).then_inc(mix1_split, 1)
            dve.wait_ge(mix1_split, 1)
            nc.vector.tensor_copy(mix1[0:64], mix1_hi[0:64].bitcast(f32)).then_inc(mix1_split, 1)
            nc.vector.tensor_tensor(mix1[64:P], mix1_raw[64:P], mix1_hi[64:P].bitcast(f32),
                                    ALU.subtract).then_inc(mix1_split, 1)
            nc.vector.tensor_scalar(x1_bias_at[:], x1_keep[:], x1_bias[:, 0:1], None, ALU.mult
                                    ).then_inc(tables_ready, 1)
            nc.vector.tensor_scalar(c1_bias_at[:], c1_keep[:], c1_bias[:, 0:1], None, ALU.mult
                                    ).then_inc(tables_ready, 1)
            dve.wait_ge(cleared, 2 * RING)
            steps(dve, step)


def wide(ap):
    return ap.rearrange("p (s w) -> p s w", s=SIDE)


def shifted(w):
    m = np.zeros((TAPS, 2, CH, 2, 2, CH), w.dtype)
    for part in range(2):
        for ri in range(2):
            for ro in range(2):
                kh = 2 * part + ri - ro
                if 0 <= kh < TAPS:
                    m[:, ri, :, part, ro, :] = w[:, :, kh, :].transpose(2, 1, 0)
    return m.reshape(SHIFTED, 2, QUAD)


def kernel(x, L0_conv_conv_w, L0_conv_w1, L0_conv_b1, L0_conv_w2, L0_conv_b2,
           L1_conv_w1, L1_conv_b1, L1_conv_w2, L1_conv_b2):
    import concourse.bacc as bacc
    from concourse.bass_utils import run_bass_kernel_spmd
    f = np.float32
    x, cw, w1, b1, w2, b2, d1, e1, d2, e2 = (np.asarray(a) for a in (
        x, L0_conv_conv_w, L0_conv_w1, L0_conv_b1, L0_conv_w2, L0_conv_b2,
        L1_conv_w1, L1_conv_b1, L1_conv_w2, L1_conv_b2))

    tall = np.zeros((1 + PAIRS * PITCH + 8, CH, SIDE, WP), f)
    body = tall[1:1 + PAIRS * PITCH].reshape(PAIRS, PITCH, CH, SIDE, WP)
    body[:, :H, :, :, 1:1 + W] = x.reshape(PAIRS, SIDE, CH, H, W).transpose(0, 3, 2, 1, 4)

    conv2 = np.zeros((P, 2, QUAD), f)
    conv2[:SHIFTED], conv2[SHIFTED:, 0] = shifted(d2), np.eye(QUAD, dtype=f)
    mix1 = np.zeros((P, 2, HIDDEN), f)
    for at in range(0, P, QUAD):
        for k in range(2):
            mix1[at + k * CH:at + (k + 1) * CH, k] = w1.T
    mix2 = np.zeros((P, 2, QUAD), f)
    for k in range(2):
        mix2[:, k, k * CH:(k + 1) * CH] = w2.T

    inside = np.arange(BLOCKS * ROWS).reshape(BLOCKS, ROWS) % PITCH
    x1_mask = np.zeros((P, BLOCKS), f)
    x1_mask[:NEW] = np.repeat((inside < H).T, CH, 0)
    inside = (np.arange(BLOCKS * ROWS).reshape(BLOCKS, ROWS) - 1) % PITCH
    c1_mask = np.zeros((P, BLOCKS), f)
    c1_mask[QUAD:] = np.repeat((inside < H).T, CH, 0)

    arrays = {
        "xt": tall.reshape(-1, SIDE * WP),
        "conv0_w": shifted(cw),
        "conv1_w": shifted(d1),
        "conv2_w": conv2,
        "mix1_w": mix1, "mix2_w": mix2,
        "mix1_b": b1.reshape(P, 1),
        "x1_b": np.tile(b2, 8).reshape(P, 1), "c1_b": np.tile(e1, 8).reshape(P, 1),
        "out_b": np.tile(e2, 8).reshape(P, 1),
        "x1_mask": x1_mask, "c1_mask": c1_mask,
    }
    nc = bacc.Bacc("TRN2", target_bir_lowering=False, num_devices=1)
    args = {}
    for name, a in arrays.items():
        arrays[name] = a = np.ascontiguousarray(a)
        args[name] = nc.dram_tensor(name, a.shape, mybir.dt.from_np(a.dtype), kind="ExternalInput").ap()
    out = nc.dram_tensor("out", (BLOCKS * NEW, COLS), mybir.dt.float32, kind="ExternalOutput").ap()
    build_program(nc, out=out, **args)
    r = run_bass_kernel_spmd(nc, [arrays], core_ids=[0])
    got = np.asarray(r.results[0]["out"]).reshape(BLOCKS * ROWS, CH, SIDE, W)
    got = got.reshape(PAIRS, PITCH, CH, SIDE, W)[:, 2:].transpose(0, 3, 2, 1, 4)
    return np.ascontiguousarray(got).reshape(IMAGES, CH, H, W)
```
